# Optimizing a Trainium2 kernel written in Bass

```python
import numpy as np
import jax
import jax.numpy as jnp

def _softmax(x, axis=-1):
    return jax.nn.softmax(x, axis=axis)

def _gelu(x):
    return jax.nn.gelu(x, approximate=True)

def _silu(x):
    return jax.nn.silu(x)

def _sigmoid(x):
    return jax.nn.sigmoid(x)

def _layernorm(x, axis=-1, eps=1e-05):
    m = jnp.mean(x, axis=axis, keepdims=True)
    v = jnp.var(x, axis=axis, keepdims=True)
    return (x - m) / jnp.sqrt(v + eps)

def _scatter_add(tgt, idx, src, axis=0):
    return tgt.at[idx].add(src)

def _segment_sum(src, seg, n):
    return jax.ops.segment_sum(src, seg, n)
kernel_name = 'mk_dlrm_tower_d1_rec_r8_993cc0'

def setup_inputs(seed: int=0):
    np.random.seed(seed)
    _w = jnp.asarray

    def _rec_inputs():
        import jax
        import jax.numpy as jnp
        _tk = jax.random.key(seed)
        ids = jnp.stack([jax.random.randint(jax.random.fold_in(_tk, 200 + f), (512,), 0, v, jnp.int32) for f, v in enumerate([1000, 1250, 125000, 1250, 1250, 1000, 12500, 1250, 12500, 12500, 12500, 1000, 1250, 1250, 1250, 12500, 1000, 1000, 1250, 1000, 1000, 1000, 1250, 12500, 12500, 1000])], axis=1)
        tbl_0 = 0.05 * jax.random.normal(jax.random.fold_in(_tk, 500 + 0), (1000, 128), jnp.float32)
        tbl_1 = 0.05 * jax.random.normal(jax.random.fold_in(_tk, 500 + 1), (1250, 128), jnp.float32)
        tbl_2 = 0.05 * jax.random.normal(jax.random.fold_in(_tk, 500 + 2), (125000, 128), jnp.float32)
        tbl_3 = 0.05 * jax.random.normal(jax.random.fold_in(_tk, 500 + 3), (1250, 128), jnp.float32)
        tbl_4 = 0.05 * jax.random.normal(jax.random.fold_in(_tk, 500 + 4), (1250, 128), jnp.float32)
        tbl_5 = 0.05 * jax.random.normal(jax.random.fold_in(_tk, 500 + 5), (1000, 128), jnp.float32)
        tbl_6 = 0.05 * jax.random.normal(jax.random.fold_in(_tk, 500 + 6), (12500, 128), jnp.float32)
        tbl_7 = 0.05 * jax.random.normal(jax.random.fold_in(_tk, 500 + 7), (1250, 128), jnp.float32)
        tbl_8 = 0.05 * jax.random.normal(jax.random.fold_in(_tk, 500 + 8), (12500, 128), jnp.float32)
        tbl_9 = 0.05 * jax.random.normal(jax.random.fold_in(_tk, 500 + 9), (12500, 128), jnp.float32)
        tbl_10 = 0.05 * jax.random.normal(jax.random.fold_in(_tk, 500 + 10), (12500, 128), jnp.float32)
        tbl_11 = 0.05 * jax.random.normal(jax.random.fold_in(_tk, 500 + 11), (1000, 128), jnp.float32)
        tbl_12 = 0.05 * jax.random.normal(jax.random.fold_in(_tk, 500 + 12), (1250, 128), jnp.float32)
        tbl_13 = 0.05 * jax.random.normal(jax.random.fold_in(_tk, 500 + 13), (1250, 128), jnp.float32)
        tbl_14 = 0.05 * jax.random.normal(jax.random.fold_in(_tk, 500 + 14), (1250, 128), jnp.float32)
        tbl_15 = 0.05 * jax.random.normal(jax.random.fold_in(_tk, 500 + 15), (12500, 128), jnp.float32)
        tbl_16 = 0.05 * jax.random.normal(jax.random.fold_in(_tk, 500 + 16), (1000, 128), jnp.float32)
        tbl_17 = 0.05 * jax.random.normal(jax.random.fold_in(_tk, 500 + 17), (1000, 128), jnp.float32)
        tbl_18 = 0.05 * jax.random.normal(jax.random.fold_in(_tk, 500 + 18), (1250, 128), jnp.float32)
        tbl_19 = 0.05 * jax.random.normal(jax.random.fold_in(_tk, 500 + 19), (1000, 128), jnp.float32)
        tbl_20 = 0.05 * jax.random.normal(jax.random.fold_in(_tk, 500 + 20), (1000, 128), jnp.float32)
        tbl_21 = 0.05 * jax.random.normal(jax.random.fold_in(_tk, 500 + 21), (1000, 128), jnp.float32)
        tbl_22 = 0.05 * jax.random.normal(jax.random.fold_in(_tk, 500 + 22), (1250, 128), jnp.float32)
        tbl_23 = 0.05 * jax.random.normal(jax.random.fold_in(_tk, 500 + 23), (12500, 128), jnp.float32)
        tbl_24 = 0.05 * jax.random.normal(jax.random.fold_in(_tk, 500 + 24), (12500, 128), jnp.float32)
        tbl_25 = 0.05 * jax.random.normal(jax.random.fold_in(_tk, 500 + 25), (1000, 128), jnp.float32)
        _rk = jax.random.fold_in(_tk, 7)
        r_dense_features = -0.000520686 + 1.00062 * jax.random.normal(jax.random.fold_in(_rk, 101), (512, 128), jnp.float32)
        W_top1 = 0.0405887 * jax.random.normal(jax.random.fold_in(_tk, 801), (607, 512), jnp.float32)
        W_top2 = 0.0441942 * jax.random.normal(jax.random.fold_in(_tk, 802), (512, 256), jnp.float32)
        W_top3 = 0.0625 * jax.random.normal(jax.random.fold_in(_tk, 803), (256, 1), jnp.float32)
        b_top1 = jnp.zeros((512,), jnp.float32)
        b_top2 = jnp.zeros((256,), jnp.float32)
        return (r_dense_features, ids, tbl_0, tbl_1, tbl_2, tbl_3, tbl_4, tbl_5, tbl_6, tbl_7, tbl_8, tbl_9, tbl_10, tbl_11, tbl_12, tbl_13, tbl_14, tbl_15, tbl_16, tbl_17, tbl_18, tbl_19, tbl_20, tbl_21, tbl_22, tbl_23, tbl_24, tbl_25, W_top1, b_top1, W_top2, b_top2, W_top3)
    r_dense_features, ids, tbl_0, tbl_1, tbl_2, tbl_3, tbl_4, tbl_5, tbl_6, tbl_7, tbl_8, tbl_9, tbl_10, tbl_11, tbl_12, tbl_13, tbl_14, tbl_15, tbl_16, tbl_17, tbl_18, tbl_19, tbl_20, tbl_21, tbl_22, tbl_23, tbl_24, tbl_25, W_top1, b_top1, W_top2, b_top2, W_top3 = _rec_inputs()

    def _L0_rec_setup():
        import jax, jax.numpy as jnp
        import numpy as np
        F = 26
        N = F + 1
        _TRIU_I, _TRIU_J = np.triu_indices(N, k=1)
        key = jax.random.key(seed)
        k1, k2 = jax.random.split(key)
        B, D = (2048, 128)
        dense_features = jax.random.normal(k1, (B, D), dtype=jnp.float32)
        sparse_features = jax.random.normal(k2, (B, F, D), dtype=jnp.float32)
        return {'dense_features': dense_features, 'sparse_features': sparse_features}
    _L0_rec_all = _L0_rec_setup()
    _L0_rec_in = {k: v for k, v in _L0_rec_all.items() if k in ()}
    del _L0_rec_all
    return {'r_dense_features': r_dense_features, 'ids': ids, 'tbl_0': tbl_0, 'tbl_1': tbl_1, 'tbl_2': tbl_2, 'tbl_3': tbl_3, 'tbl_4': tbl_4, 'tbl_5': tbl_5, 'tbl_6': tbl_6, 'tbl_7': tbl_7, 'tbl_8': tbl_8, 'tbl_9': tbl_9, 'tbl_10': tbl_10, 'tbl_11': tbl_11, 'tbl_12': tbl_12, 'tbl_13': tbl_13, 'tbl_14': tbl_14, 'tbl_15': tbl_15, 'tbl_16': tbl_16, 'tbl_17': tbl_17, 'tbl_18': tbl_18, 'tbl_19': tbl_19, 'tbl_20': tbl_20, 'tbl_21': tbl_21, 'tbl_22': tbl_22, 'tbl_23': tbl_23, 'tbl_24': tbl_24, 'tbl_25': tbl_25, 'W_top1': W_top1, 'b_top1': b_top1, 'W_top2': W_top2, 'b_top2': b_top2, 'W_top3': W_top3}

def reference(r_dense_features, ids, tbl_0, tbl_1, tbl_2, tbl_3, tbl_4, tbl_5, tbl_6, tbl_7, tbl_8, tbl_9, tbl_10, tbl_11, tbl_12, tbl_13, tbl_14, tbl_15, tbl_16, tbl_17, tbl_18, tbl_19, tbl_20, tbl_21, tbl_22, tbl_23, tbl_24, tbl_25, W_top1, b_top1, W_top2, b_top2, W_top3):
    import jax
    import jax.numpy as jnp

    def _L0_rec_ref(dense_features, sparse_features):
        import jax, jax.numpy as jnp
        import numpy as np
        F = 26
        N = F + 1
        _TRIU_I, _TRIU_J = np.triu_indices(N, k=1)
        combined = jnp.concatenate([dense_features[:, None, :], sparse_features], axis=1)
        interactions = jnp.einsum('bnd,bmd->bnm', combined, combined)
        interactions_flat = interactions[:, _TRIU_I, _TRIU_J]
        return jnp.concatenate([dense_features, interactions_flat], axis=1)
    e = jnp.stack([tbl_0[ids[:, 0]], tbl_1[ids[:, 1]], tbl_2[ids[:, 2]], tbl_3[ids[:, 3]], tbl_4[ids[:, 4]], tbl_5[ids[:, 5]], tbl_6[ids[:, 6]], tbl_7[ids[:, 7]], tbl_8[ids[:, 8]], tbl_9[ids[:, 9]], tbl_10[ids[:, 10]], tbl_11[ids[:, 11]], tbl_12[ids[:, 12]], tbl_13[ids[:, 13]], tbl_14[ids[:, 14]], tbl_15[ids[:, 15]], tbl_16[ids[:, 16]], tbl_17[ids[:, 17]], tbl_18[ids[:, 18]], tbl_19[ids[:, 19]], tbl_20[ids[:, 20]], tbl_21[ids[:, 21]], tbl_22[ids[:, 22]], tbl_23[ids[:, 23]], tbl_24[ids[:, 24]], tbl_25[ids[:, 25]]], axis=1)
    z = _L0_rec_ref(r_dense_features, e)
    z = z.reshape(z.shape[0], -1)
    h = jnp.concatenate([z, r_dense_features], axis=1)
    h = jnp.maximum(h @ W_top1 + b_top1, 0.0)
    h = jnp.maximum(h @ W_top2 + b_top2, 0.0)
    y = h @ W_top3
    return y

_drawn_inputs = setup_inputs


def setup_inputs(seed=0):
    import zlib

    import numpy as np

    out = dict(_drawn_inputs(seed))
    spreads = {'b_top1': (0.0, 0.1), 'b_top2': (0.0, 0.1)}
    factors = {}
    for name, (base, spread) in spreads.items():
        noise = np.random.default_rng([zlib.crc32(name.encode()), seed]).standard_normal(out[name].shape)
        drawn = base * np.exp(spread * noise) if base else spread * noise
        out[name] = jnp.asarray(drawn.astype(out[name].dtype))
    for name, factor in factors.items():
        out[name] = (out[name] * factor).astype(out[name].dtype)
    return out
```

```python
from contextlib import ExitStack

import concourse.bass as bass
from concourse import mybir

F32 = mybir.dt.float32
BF16 = mybir.dt.bfloat16
F16 = mybir.dt.float16
I32 = mybir.dt.int32
ALU = mybir.AluOpType
ACT = mybir.ActivationFunctionType

P = 128
LOOKUP = [0, 16, 17, 19, 20, 21]
BANK = 512
SLOTS = 32
PACK = P // SLOTS
FILL_GROUPS = 3


def gather_groups(n_tables):
    groups = []
    for f in range(n_tables):
        if f in LOOKUP:
            continue
        if groups and groups[-1][-1] == f - 1 and len(groups[-1]) < BANK // P:
            groups[-1].append(f)
        else:
            groups.append([f])
    return sorted(groups, key=lambda g: -len(g))


def build(nc, dense, ids, ids_by_table, tables, W1, b1, W2, b2, W3, out):
    B, D = dense.shape
    NF = len(tables)
    N = NF + 1
    TILES = B // P
    PACKS = P // PACK
    PAIRS = N * (N - 1) // 2
    NCH = 3
    CH = PAIRS // NCH
    H1, H2 = W1.shape[1], W2.shape[1]
    K1, K2 = H1 // P, H2 // P
    GROUPS = gather_groups(NF)
    NG = len(GROUPS)
    GATHERED = [f for g in GROUPS for f in g]
    COL = {f: i for i, f in enumerate(GATHERED)}
    NL = len(LOOKUP)
    ROWS = tables[LOOKUP[0]].shape[0]
    RCH = -(-ROWS // P)
    RP = ROWS // RCH
    RING = 3
    CBANK = BANK // P
    CB = -(-(N - 1) // CBANK)
    GB = PACKS // CBANK
    ZUSES = CB + 1
    NC = K1 + K2 + K2
    assert CH * NCH == PAIRS and RP * RCH == ROWS and ZUSES % 2 == 0 and PACKS == SLOTS and K2 == 2
    pair_at = [c * N - c * (c + 1) // 2 for c in range(N)]

    with ExitStack() as ctx:
        def sb(name, shape, dt):
            return ctx.enter_context(nc.sbuf_tensor(name, shape, dt))

        def banks(name, n):
            return [ctx.enter_context(nc.psum_tensor(f"{name}{i}", [P, BANK], F32)) for i in range(n)]

        def sem(name):
            return ctx.enter_context(nc.semaphore(name))

        ident = sb("ident", [P, P], F32)
        idx = sb("idx", [P, TILES, NF], I32)
        emb = sb("emb", [P, 2, len(GATHERED), D], F32)
        dense_sb = sb("dense_sb", [P, TILES, D], F32)
        xt = sb("xt", [P, B, SLOTS], F32)
        dense_t = sb("dense_t", [P, B], F32)
        rowid_i = sb("rowid_i", [P, RCH], I32)
        rowid = sb("rowid", [P, RCH], F32)
        want_i = sb("want_i", [RP, NL, B], I32)
        want = sb("want", [RP, NL, B], F16)
        table = sb("table", [RP, NL, RCH * D], F32)
        part = [sb(f"part{k}", [RP, RING, RCH * D], BF16) for k in range(3)]
        hot = sb("hot", [RP, RING, RCH, B], BF16)
        gram = sb("gram", [P, N - 1, PACKS], F32)
        z = sb("z", [PACKS, PACK, PAIRS], F32)
        zt = sb("zt", [CH, NCH, P], F32)
        w1a = sb("w1a", [P, H1], F32)
        w1z = sb("w1z", [CH, NCH, H1], F32)
        w1d = sb("w1d", [P, H1], F32)
        w2 = sb("w2", [P, K1, H2], F32)
        small = sb("small", [NC, P], F32)
        cols = sb("cols", [P, NC], F32)
        h1 = sb("h1", [P, K1, P], F32)
        h2 = sb("h2", [P, K2, P], F32)
        y = sb("y", [1, B], F32)

        tr_ps = banks("tr_ps", 2)
        gram_ps = banks("gram_ps", 2)
        sp_ps = banks("sp_ps", 2)
        mm_ps = banks("mm_ps", 2)

        b1_col, b2_col, w3_col = cols[:, 0:K1], cols[:, K1:K1 + K2], cols[:, K1 + K2:NC]

        s_idx = sem("s_idx")
        s_want = sem("s_want")
        s_dense = sem("s_dense")
        s_small = sem("s_small")
        s_w1 = sem("s_w1")
        s_w2 = sem("s_w2")
        s_out = sem("s_out")
        s_table = [sem(f"s_table{o}") for o in range(NL)]
        s_emb = [[sem(f"s_emb{t}_{g}") for g in range(NG)] for t in range(TILES)]
        s_zero = sem("s_zero")
        s_ident = sem("s_ident")
        s_iota = sem("s_iota")
        s_pad = sem("s_pad")
        s_rowid = sem("s_rowid")
        s_cast = sem("s_cast")
        s_part0 = sem("s_part0")
        s_rest = sem("s_rest")
        s_part1 = sem("s_part1")
        s_part2 = sem("s_part2")
        s_look = sem("s_look")
        s_lcopy = sem("s_lcopy")
        s_tr = sem("s_tr")
        s_trv = sem("s_trv")
        s_tra = sem("s_tra")
        s_gram = sem("s_gram")
        s_gv = sem("s_gv")
        s_ga = sem("s_ga")
        s_sp = sem("s_sp")
        s_spv = sem("s_spv")
        s_spa = sem("s_spa")
        s_l1 = sem("s_l1")
        s_l2 = sem("s_l2")
        s_l3 = sem("s_l3")
        s_h1v = sem("s_h1v")
        s_h1a = sem("s_h1a")
        s_h2v = sem("s_h2v")
        s_h2a = sem("s_h2a")
        s_y = sem("s_y")

        FIRST = 2
        NLC = min(NL, NG)

        def tr_use(t, g):
            return FIRST + t * NG + g

        def layer1_ps(m):
            return mm_ps[m // (K1 // 2)][:, m % (K1 // 2) * P:(m % (K1 // 2) + 1) * P]

        def layer2_ps(m):
            return mm_ps[m][:, 0:P]

        layer3_ps = mm_ps[1][0:1, P:2 * P]

        def group_to_xt(copy, t, g):
            n, f = len(GROUPS[g]), GROUPS[g][0] + 1
            return copy(xt[:, t * P:(t + 1) * P, f:f + n].rearrange("p s f -> p f s"),
                        tr_ps[tr_use(t, g) % 2][:, 0:n * P].rearrange("p (f s) -> p f s", f=n))

        def gram_to_sb(copy, t, q, j):
            quad = slice(j * SLOTS, (j + 1) * SLOTS)
            src = gram_ps[(t * GB + q) % 2][quad, :].rearrange("p (i n) -> p i n", i=CBANK)
            return copy(gram[quad, :, q * CBANK:(q + 1) * CBANK].rearrange("p c i -> p i c"),
                        src[:, :, j * (N - 1):(j + 1) * (N - 1)])

        def column_to_z(copy, t, c):
            u = t * ZUSES + c // CBANK
            src = sp_ps[u % 2][0:PACKS, (c % CBANK) * P:(c % CBANK + 1) * P].rearrange("p (j r) -> p j r", j=PACK)
            return copy(z[:, :, pair_at[c]:pair_at[c] + N - 1 - c], src[:, :, c + 1:N])

        block = ctx.enter_context(nc.Block())

        @block.sync
        def _(sp):
            sp.dma_start(idx[:], ids.rearrange("(t p) f -> p t f", p=P)).then_inc(s_idx, 16)
            full = RP // 16 * 16
            for o in range(NL):
                rows = tables[LOOKUP[o]].rearrange("(p c) d -> p (c d)", c=RCH)
                sp.dma_start(table[0:full, o, :], rows[0:full]).then_inc(s_table[o], 16)
                sp.dma_start(table[full:RP, o, :], rows[full:RP]).then_inc(s_table[o], 16)
                if o == 0:
                    sp.dma_start(dense_sb[:], dense.rearrange("(t p) d -> p t d", p=P)).then_inc(s_dense, 16)
                    sp.dma_start(small[0:K1, :], b1.rearrange("(k p) -> k p", p=P)).then_inc(s_small, 16)
                    sp.dma_start(small[K1:K1 + K2, :], b2.rearrange("(k p) -> k p", p=P)).then_inc(s_small, 16)
                    sp.dma_start(small[K1 + K2:NC, :],
                                 W3.rearrange("(k p) o -> k (p o)", p=P)).then_inc(s_small, 16)
            sp.dma_start(w1a[:], W1[0:D, :]).then_inc(s_w1, 16)
            sp.dma_start(w1d[:], W1[D + PAIRS:2 * D + PAIRS, :]).then_inc(s_w1, 16)
            sp.dma_start(w1z[:], W1[D:D + PAIRS, :].rearrange("(k p) n -> p k n", p=CH)).then_inc(s_w1, 16)
            sp.dma_start(w2[:], W2.rearrange("(k p) n -> p k n", p=P)).then_inc(s_w2, 16)
            sp.wait_ge(s_y, TILES)
            sp.dma_start(out.rearrange("b o -> o b"), y[:]).then_inc(s_out, 16)
            sp.wait_ge(s_out, 16)

        @block.gpsimd
        def _(pool):
            nc.gpsimd.memset(ident[:], 0.0).then_inc(s_zero, 1)
            nc.gpsimd.iota(rowid_i[:], pattern=[[1, RCH]], base=0, channel_multiplier=RCH).then_inc(s_iota, 1)
            pool.wait_ge(s_zero, 1)
            nc.gpsimd.affine_select(out=ident[:], in_=ident[:], compare_op=ALU.not_equal, fill=1.0, base=0,
                                    pattern=[[-1, P]], channel_multiplier=1).then_inc(s_ident, 1)
            pool.wait_ge(s_idx, 16)
            for t in range(TILES):
                for g, group in enumerate(GROUPS):
                    if t >= 2:
                        pool.wait_ge(s_tr, tr_use(t - 2, g) + 1)
                    for f in group:
                        nc.gpsimd.indirect_dma_start(
                            out=emb[:, t % 2, COL[f], :], out_offset=None, in_=tables[f],
                            in_offset=bass.IndirectOffsetOnAxis(ap=idx[:, t, f:f + 1], axis=0),
                        ).then_inc(s_emb[t][g], 16)

        @block.tensor
        def _(pe):
            def inputs():
                pe.wait_ge(s_ident, 1)
                pe.wait_ge(s_dense, 16)
                for t in range(TILES):
                    last = nc.tensor.transpose(tr_ps[0][:, t * P:(t + 1) * P], dense_sb[:, t, :], ident[:])
                last.then_inc(s_tr, 1)
                pe.wait_ge(s_small, 48)
                nc.tensor.transpose(tr_ps[1][:, 0:NC], small[:], ident[0:NC, 0:NC]).then_inc(s_tr, 1)

            def lookup(o):
                pe.wait_ge(s_part2, o + 1)
                pe.wait_ge(s_part1, o + 1)
                if o >= 2:
                    pe.wait_ge(s_lcopy, o - 1)
                for c in range(RCH):
                    for k in range(3):
                        last = nc.tensor.matmul(mm_ps[o % 2][:, 0:B], part[k][:, o % RING, c * D:(c + 1) * D],
                                                hot[:, o % RING, c, :], start=(c == 0 and k == 0),
                                                stop=(c == RCH - 1 and k == 2))
                last.then_inc(s_look, 1)

            def group(t, g):
                u = tr_use(t, g)
                pe.wait_ge(s_emb[t][g], 16 * len(GROUPS[g]))
                pe.wait_ge(s_tra if u % 2 else s_trv, u // 2)
                for i, f in enumerate(GROUPS[g]):
                    last = nc.tensor.transpose(tr_ps[u % 2][:, i * P:(i + 1) * P], emb[:, t % 2, COL[f], :],
                                               ident[:])
                last.then_inc(s_tr, 1)

            def gram_bank(t, q):
                u = t * GB + q
                if u >= 2:
                    pe.wait_ge(s_gv, u - 1)
                    pe.wait_ge(s_ga, u - 1)
                for i in range(CBANK):
                    s = t * P + (q * CBANK + i) * PACK
                    last = nc.tensor.matmul(
                        gram_ps[u % 2][:, i * P:i * P + PACK * (N - 1)].rearrange("p (s n) -> p s n", s=PACK),
                        xt[:, s:s + PACK, :].rearrange("p s n -> p (s n)"), xt[:, s:s + PACK, 0:N - 1],
                        start=True, stop=True)
                last.then_inc(s_gram, 1)

            def gram_tile(t):
                u = tr_use(t, NG - 1)
                pe.wait_ge(s_trv, u // 2 + 1 if u % 2 == 0 else (u - 1) // 2 + 1)
                pe.wait_ge(s_tra, (u + 1) // 2)
                pe.wait_ge(s_lcopy, NL)
                pe.wait_ge(s_pad, 1)
                for q in range(GB):
                    gram_bank(t, q)

            def spread(t):
                pe.wait_ge(s_gv, GB * (t + 1))
                pe.wait_ge(s_ga, GB * (t + 1))
                for b in range(CB):
                    u = t * ZUSES + b
                    pe.wait_ge(s_spa if u % 2 else s_spv, u // 2)
                    for c in range(b * CBANK, min(N - 1, (b + 1) * CBANK)):
                        last = nc.tensor.transpose(sp_ps[u % 2][0:PACKS, (c % CBANK) * P:(c % CBANK + 1) * P],
                                                   gram[:, c, :], ident[:])
                    last.then_inc(s_sp, 1)

            def pairs(t):
                u = t * ZUSES + CB
                pe.wait_ge(s_spv, (u + 1) // 2)
                pe.wait_ge(s_spa, u // 2)
                for k in range(NCH):
                    for j in range(PACK):
                        at = k * P + j * PACKS
                        last = nc.tensor.transpose(sp_ps[u % 2][0:CH, at:at + PACKS],
                                                   z[:, j, k * CH:(k + 1) * CH], ident[0:PACKS, 0:PACKS])
                last.then_inc(s_sp, 1)

            def layer1_dense(t):
                if t == 0:
                    pe.wait_ge(s_w1, 48)
                    pe.wait_ge(s_lcopy, NL)
                else:
                    pe.wait_ge(s_y, t)
                for m in range(K1):
                    for w in (w1a, w1d):
                        nc.tensor.matmul(layer1_ps(m), w[:, m * P:(m + 1) * P],
                                         dense_t[:, t * P:(t + 1) * P],
                                         start=(m % (K1 // 2) == 0 and w is w1a),
                                         stop=False, skip_group_check=True)

            def layer1_pairs(t):
                pe.wait_ge(s_spa, (t + 1) * ZUSES // 2)
                for m in range(K1):
                    for k in range(NCH):
                        last = nc.tensor.matmul(layer1_ps(m), w1z[:, k, m * P:(m + 1) * P],
                                                zt[:, k, :], start=False, stop=(k == NCH - 1),
                                                skip_group_check=True)
                last.then_inc(s_l1, 1)

            def layer2(t):
                if t == 0:
                    pe.wait_ge(s_w2, 16)
                pe.wait_ge(s_h1v, t + 1)
                pe.wait_ge(s_h1a, t + 1)
                for m in range(K2):
                    for k in range(K1):
                        last = nc.tensor.matmul(layer2_ps(m), w2[:, k, m * P:(m + 1) * P],
                                                h1[:, k, :], start=(k == 0), stop=(k == K1 - 1))
                last.then_inc(s_l2, 1)

            def layer3(t):
                pe.wait_ge(s_h2v, t + 1)
                pe.wait_ge(s_h2a, t + 1)
                for k in range(K2):
                    last = nc.tensor.matmul(layer3_ps, w3_col[:, k:k + 1],
                                            h2[:, k, :], start=(k == 0), stop=(k == K2 - 1))
                last.then_inc(s_l3, 1)

            inputs()
            for o in range(NL):
                lookup(o)
                if o < NG:
                    group(0, o)
            for g in range(NL, NG):
                group(0, g)
            for t in range(TILES):
                more = list(range(FILL_GROUPS)) if t + 1 < TILES else []
                gram_tile(t)
                layer1_dense(t)
                spread(t)
                if more:
                    group(t + 1, more.pop(0))
                pairs(t)
                if more:
                    group(t + 1, more.pop(0))
                layer1_pairs(t)
                if more:
                    group(t + 1, more.pop(0))
                layer2(t)
                layer3(t)
                if t + 1 < TILES:
                    for g in range(FILL_GROUPS, NG):
                        group(t + 1, g)

        @block.vector
        def _(dve):
            def rows():
                dve.wait_ge(s_iota, 1)
                nc.vector.tensor_copy(rowid[:], rowid_i[:]).then_inc(s_rowid, 1)
                dve.wait_ge(s_rowid, 1)

            def build(o):
                dve.wait_ge(s_part0, o + 1)
                if o >= RING:
                    dve.wait_ge(s_look, o - RING + 1)
                tab = table[:, o, :]
                nc.vector.tensor_tensor(tab, tab, part[0][:, o % RING, :], ALU.subtract).then_inc(s_rest, 1)
                dve.wait_ge(s_cast, o + 1)
                for c in range(RCH):
                    nc.vector.tensor_scalar(hot[:, o % RING, c, :], want[:, o, :], rowid[0:RP, c:c + 1], None,
                                            ALU.is_equal)
                dve.wait_ge(s_part1, o + 1)
                nc.vector.tensor_tensor(part[2][:, o % RING, :], tab, part[1][:, o % RING, :],
                                        ALU.subtract).then_inc(s_part2, 1)

            def dense_copy():
                dve.wait_ge(s_tr, 1)
                nc.vector.tensor_copy(xt[:, :, 0], tr_ps[0][:, 0:B])
                nc.vector.tensor_copy(dense_t[:], tr_ps[0][:, 0:B]).then_inc(s_trv, 1)

            def group_copy(t, g):
                u = tr_use(t, g)
                if u % 2 == 0:
                    dve.wait_ge(s_tr, u + 1)
                    group_to_xt(nc.vector.tensor_copy, t, g).then_inc(s_trv, 1)

            def gram_copy(t):
                for q in range(GB):
                    dve.wait_ge(s_gram, t * GB + q + 1)
                    for j in range(PACK // 2):
                        last = gram_to_sb(nc.vector.tensor_copy, t, q, j)
                    last.then_inc(s_gv, 1)

            def spread_copy(t):
                for b in range(0, CB, 2):
                    dve.wait_ge(s_sp, t * ZUSES + b + 1)
                    for c in range(b * CBANK, min(N - 1, (b + 1) * CBANK)):
                        last = column_to_z(nc.vector.tensor_copy, t, c)
                    last.then_inc(s_spv, 1)

            def relu(out_, in_, bias):
                return nc.vector.tensor_scalar(out_, in_, bias, 0.0, ALU.add, ALU.max)

            def layer1_relu(t):
                if t == 0:
                    dve.wait_ge(s_tra, 1)
                dve.wait_ge(s_l1, t + 1)
                for m in range(K1 // 2):
                    last = relu(h1[:, m, :], layer1_ps(m), b1_col[:, m:m + 1])
                last.then_inc(s_h1v, 1)

            def layer2_relu(t):
                dve.wait_ge(s_l2, t + 1)
                for m in range(K2 // 2):
                    last = relu(h2[:, m, :], layer2_ps(m), b2_col[:, m:m + 1])
                last.then_inc(s_h2v, 1)

            nc.vector.memset(xt[:, :, N:SLOTS], 0.0).then_inc(s_pad, 1)
            rows()
            build(0)
            dense_copy()
            for o in range(NL):
                if o + 1 < NL:
                    build(o + 1)
                if o < NG:
                    group_copy(0, o)
            for g in range(NL, NG):
                group_copy(0, g)
            for t in range(TILES):
                more = list(range(FILL_GROUPS)) if t + 1 < TILES else []
                gram_copy(t)
                spread_copy(t)
                if more:
                    group_copy(t + 1, more.pop(0))
                if more:
                    group_copy(t + 1, more.pop(0))
                layer1_relu(t)
                if more:
                    group_copy(t + 1, more.pop(0))
                layer2_relu(t)
                if t + 1 < TILES:
                    for g in range(FILL_GROUPS, NG):
                        group_copy(t + 1, g)

        @block.scalar
        def _(act):
            def cast(o):
                if o == 0:
                    act.wait_ge(s_want, 16)
                nc.scalar.copy(want[:, o, :], want_i[:, o, :]).then_inc(s_cast, 1)

            def build(o):
                act.wait_ge(s_table[o], 32)
                if o >= RING:
                    act.wait_ge(s_look, o - RING + 1)
                nc.scalar.copy(part[0][:, o % RING, :], table[:, o, :]).then_inc(s_part0, 1)
                cast(o)
                act.wait_ge(s_rest, o + 1)
                nc.scalar.copy(part[1][:, o % RING, :], table[:, o, :]).then_inc(s_part1, 1)

            def lookup_copy(o):
                act.wait_ge(s_look, o + 1)
                nc.scalar.copy(xt[:, :, LOOKUP[o] + 1], mm_ps[o % 2][:, 0:B]).then_inc(s_lcopy, 1)

            def group_copy(t, g):
                u = tr_use(t, g)
                if u % 2 == 1:
                    act.wait_ge(s_tr, u + 1)
                    group_to_xt(nc.scalar.copy, t, g).then_inc(s_tra, 1)

            def gram_copy(t):
                for q in range(GB):
                    act.wait_ge(s_gram, t * GB + q + 1)
                    for j in range(PACK // 2, PACK):
                        last = gram_to_sb(nc.scalar.copy, t, q, j)
                    last.then_inc(s_ga, 1)

            def spread_copy(t):
                for b in range(1, CB, 2):
                    act.wait_ge(s_sp, t * ZUSES + b + 1)
                    for c in range(b * CBANK, min(N - 1, (b + 1) * CBANK)):
                        last = column_to_z(nc.scalar.copy, t, c)
                    last.then_inc(s_spa, 1)

            def pairs_copy(t):
                u = t * ZUSES + CB
                act.wait_ge(s_sp, u + 1)
                nc.scalar.copy(zt[:].rearrange("p k (q j) -> p k j q", j=PACK),
                               sp_ps[u % 2][0:CH, 0:NCH * P].rearrange("p (k j q) -> p k j q", k=NCH, j=PACK)
                               ).then_inc(s_spa, 1)

            def relu(out_, in_, bias):
                return nc.scalar.activation(out_, in_, ACT.Relu, bias=bias)

            def layer1_relu(t):
                act.wait_ge(s_l1, t + 1)
                for m in range(K1 // 2, K1):
                    last = relu(h1[:, m, :], layer1_ps(m), b1_col[:, m:m + 1])
                last.then_inc(s_h1a, 1)

            def layer2_relu(t):
                act.wait_ge(s_l2, t + 1)
                for m in range(K2 // 2, K2):
                    last = relu(h2[:, m, :], layer2_ps(m), b2_col[:, m:m + 1])
                last.then_inc(s_h2a, 1)

            def result(t):
                act.wait_ge(s_l3, t + 1)
                nc.scalar.copy(y[0:1, t * P:(t + 1) * P], layer3_ps).then_inc(s_y, 1)

            for o in range(NL):
                act.dma_start(want_i[:, o, :], ids_by_table[LOOKUP[o]].partition_broadcast(RP)
                              ).then_inc(s_want, 16)
            act.wait_ge(s_want, 16 * NL)
            build(0)
            act.wait_ge(s_tr, 2)
            nc.scalar.copy(cols[:], tr_ps[1][:, 0:NC]).then_inc(s_tra, 1)
            act.wait_ge(s_tra, 1)
            for o in range(NL):
                if o + 1 < NL:
                    build(o + 1)
                lookup_copy(o)
                if o < NG:
                    group_copy(0, o)
            for g in range(NL, NG):
                group_copy(0, g)
            for t in range(TILES):
                more = list(range(FILL_GROUPS)) if t + 1 < TILES else []
                gram_copy(t)
                spread_copy(t)
                if more:
                    group_copy(t + 1, more.pop(0))
                pairs_copy(t)
                if more:
                    group_copy(t + 1, more.pop(0))
                layer1_relu(t)
                if more:
                    group_copy(t + 1, more.pop(0))
                layer2_relu(t)
                result(t)
                if t + 1 < TILES:
                    for g in range(FILL_GROUPS, NG):
                        group_copy(t + 1, g)


N_TABLES = 26


def kernel(**inputs):
    import numpy as np
    import concourse.bacc as bacc
    from concourse.bass_utils import run_bass_kernel_spmd

    nc = bacc.Bacc("TRN2", target_bir_lowering=False, num_devices=1)
    names = ["r_dense_features", "ids"] + [f"tbl_{f}" for f in range(N_TABLES)]
    names += ["W_top1", "b_top1", "W_top2", "b_top2", "W_top3"]
    arrays = {name: np.ascontiguousarray(inputs[name]) for name in names}
    arrays["ids_by_table"] = np.ascontiguousarray(arrays["ids"].T)
    aps = {name: nc.dram_tensor(f"in_{name}", a.shape, mybir.dt.from_np(a.dtype), kind="ExternalInput").ap()
           for name, a in arrays.items()}
    out = nc.dram_tensor("out", (arrays["ids"].shape[0], 1), F32, kind="ExternalOutput").ap()
    build(nc, aps["r_dense_features"], aps["ids"], aps["ids_by_table"],
          [aps[f"tbl_{f}"] for f in range(N_TABLES)],
          aps["W_top1"], aps["b_top1"], aps["W_top2"], aps["b_top2"], aps["W_top3"], out)
    r = run_bass_kernel_spmd(nc, [{f"in_{name}": a for name, a in arrays.items()}], core_ids=[0])
    return r.results[0]["out"]
```

```python
from contextlib import ExitStack

import concourse.bass as bass
from concourse import mybir

F32 = mybir.dt.float32
BF16 = mybir.dt.bfloat16
F16 = mybir.dt.float16
I32 = mybir.dt.int32
ALU = mybir.AluOpType
ACT = mybir.ActivationFunctionType

P = 128
LOOKUP = [0, 16, 17, 19, 20]
BANK = 512
SLOTS = 32
PACK = P // SLOTS
NCH = 3
FILL_GROUPS = 3


def chunk_blocks(n_features):
    blocks, at = [], 0
    for c in range(0, n_features - 1, NCH):
        blocks.append((c, c + 1, at, n_features - 1 - c))
        at += n_features - 1 - c
    return blocks, at


def gather_groups(n_tables):
    groups = []
    for f in range(n_tables):
        if f in LOOKUP:
            continue
        if groups and groups[-1][-1] == f - 1 and len(groups[-1]) < BANK // P:
            groups[-1].append(f)
        else:
            groups.append([f])
    return sorted(groups, key=lambda g: -len(g))


def build(nc, dense, ids, lookup_ids, tables, W1, W1_pairs, b1, W2, b2, W3, out):
    B, D = dense.shape
    NF = len(tables)
    N = NF + 1
    TILES = B // P
    PACKS = P // PACK
    PAIRS = N * (N - 1) // 2
    BLOCKS, CH = chunk_blocks(N)
    H1, H2 = W1.shape[1], W2.shape[1]
    K1, K2 = H1 // P, H2 // P
    GROUPS = gather_groups(NF)
    NG = len(GROUPS)
    GATHERED = [f for g in GROUPS for f in g]
    COL = {f: i for i, f in enumerate(GATHERED)}
    NL = len(LOOKUP)
    ROWS = tables[LOOKUP[0]].shape[0]
    RCH = -(-ROWS // P)
    RP = ROWS // RCH
    WORK = 4
    RING = 3
    CBANK = BANK // P
    GB = PACKS // CBANK
    SB = -(-len(BLOCKS) // CBANK)
    COPIED_BY = ["VA"] * GB + ["VA"[b % 2] for b in range(SB)] + ["V", "A"]
    USES = len(COPIED_BY)
    NC = K1 + K2 + K2
    assert N % NCH == 0 and CH <= P and RP * RCH == ROWS and PACKS == SLOTS and K2 == 2

    with ExitStack() as ctx:
        def sb(name, shape, dt):
            return ctx.enter_context(nc.sbuf_tensor(name, shape, dt))

        def banks(name, n):
            return [ctx.enter_context(nc.psum_tensor(f"{name}{i}", [P, BANK], F32)) for i in range(n)]

        def sem(name):
            return ctx.enter_context(nc.semaphore(name))

        ident = sb("ident", [P, P], F32)
        idx = sb("idx", [P, TILES, NF], I32)
        emb = sb("emb", [P, 2, len(GATHERED), D], F32)
        dense_sb = sb("dense_sb", [P, TILES, D], F32)
        xt = sb("xt", [P, B, SLOTS], F32)
        dense_t = sb("dense_t", [P, B], F32)
        rowid_i = sb("rowid_i", [P, RCH], I32)
        rowid = sb("rowid", [P, RCH], F32)
        want_i = sb("want_i", [RP, NL, B], I32)
        want = sb("want", [RP, NL, B], F16)
        table = sb("table", [RP, NL, RCH * D], F32)
        part = [sb(f"part{k}", [RP, RING, RCH * D], BF16) for k in range(3)]
        hot = sb("hot", [RP, RING, RCH, B], BF16)
        gram = sb("gram", [P, N, PACKS], F32)
        z = sb("z", [NCH * PACKS, PACK, CH], F32)
        zt = sb("zt", [CH, NCH, P], F32)
        w1a = sb("w1a", [P, H1], F32)
        w1z = sb("w1z", [CH, NCH, H1], F32)
        w1d = sb("w1d", [P, H1], F32)
        w2 = sb("w2", [P, K1, H2], F32)
        small = sb("small", [NC, P], F32)
        cols = sb("cols", [P, NC], F32)
        h1 = sb("h1", [P, K1, P], F32)
        h2 = sb("h2", [P, K2, P], F32)
        y = sb("y", [1, B], F32)

        tr_ps = banks("tr_ps", 2)
        work_ps = banks("work_ps", WORK)
        mm_ps = banks("mm_ps", 2)

        b1_col, b2_col, w3_col = cols[:, 0:K1], cols[:, K1:K1 + K2], cols[:, K1 + K2:NC]

        s_idx = sem("s_idx")
        s_want = [sem("s_want_first"), sem("s_want_rest")]
        s_dense = sem("s_dense")
        s_small = sem("s_small")
        s_w1 = sem("s_w1")
        s_w1z = sem("s_w1z")
        s_w2 = sem("s_w2")
        s_out = sem("s_out")
        s_table = [sem(f"s_table{o}") for o in range(NL)]
        s_emb = [[sem(f"s_emb{t}_{g}") for g in range(NG)] for t in range(TILES)]
        s_zero = sem("s_zero")
        s_ident = sem("s_ident")
        s_iota = sem("s_iota")
        s_pad = sem("s_pad")
        s_rowid = sem("s_rowid")
        s_cast = sem("s_cast")
        s_part0 = sem("s_part0")
        s_rest = sem("s_rest")
        s_part1 = sem("s_part1")
        s_part2 = sem("s_part2")
        s_hot = sem("s_hot")
        s_w1sum = sem("s_w1sum")
        s_zero_col = sem("s_zero_col")
        s_look = sem("s_look")
        s_lcopy = sem("s_lcopy")
        s_tr = sem("s_tr")
        s_trv = sem("s_trv")
        s_tra = sem("s_tra")
        s_work = sem("s_work")
        s_wv = sem("s_wv")
        s_wa = sem("s_wa")
        s_l1 = sem("s_l1")
        s_l2 = sem("s_l2")
        s_l3 = sem("s_l3")
        s_h1v = sem("s_h1v")
        s_h1a = sem("s_h1a")
        s_h2v = sem("s_h2v")
        s_h2a = sem("s_h2a")
        s_y = sem("s_y")

        FIRST = 2

        def tr_use(t, g):
            return FIRST + t * NG + g

        def copies(engine, t, i):
            return t * sum(engine in e for e in COPIED_BY) + sum(engine in e for e in COPIED_BY[:i + 1])

        def work_bank(t, i):
            return work_ps[(t * USES + i) % WORK]

        def layer1_ps(m):
            return mm_ps[m // (K1 // 2)][:, m % (K1 // 2) * P:(m % (K1 // 2) + 1) * P]

        def layer2_ps(m):
            return mm_ps[m][:, 0:P]

        layer3_ps = mm_ps[1][0:1, P:2 * P]

        def group_to_xt(copy, t, g):
            n, f = len(GROUPS[g]), GROUPS[g][0] + 1
            return copy(xt[:, t * P:(t + 1) * P, f:f + n].rearrange("p s f -> p f s"),
                        tr_ps[tr_use(t, g) % 2][:, 0:n * P].rearrange("p (f s) -> p f s", f=n))

        def gram_to_sb(copy, t, q, j):
            quad = slice(j * SLOTS, (j + 1) * SLOTS)
            src = work_bank(t, q)[quad, :].rearrange("p (i n) -> p i n", i=CBANK)
            return copy(gram[quad, 0:N - 1, q * CBANK:(q + 1) * CBANK].rearrange("p c i -> p i c"),
                        src[:, :, j * (N - 1):(j + 1) * (N - 1)])

        def columns_to_z(copy, t, b):
            for i, (_, r, at, n) in enumerate(BLOCKS[b * CBANK:(b + 1) * CBANK]):
                src = work_bank(t, GB + b)[0:NCH * PACKS, i * P:(i + 1) * P].rearrange("p (j r) -> p j r", j=PACK)
                last = copy(z[:, :, at:at + n], src[:, :, r:r + n])
            return last

        def pairs_to_zt(copy, t, h):
            n = PACK // 2
            src = work_bank(t, GB + SB + h)[0:CH, 0:n * NCH * PACKS]
            return copy(zt[:].rearrange("p k (q j) -> p j k q", j=PACK)[:, h * n:(h + 1) * n],
                        src.rearrange("p (j k q) -> p j k q", j=n, k=NCH))

        block = ctx.enter_context(nc.Block())

        @block.sync
        def _(sp):
            sp.dma_start(idx[:], ids.rearrange("(t p) f -> p t f", p=P)).then_inc(s_idx, 16)
            full = RP // 16 * 16
            for o in range(NL):
                rows = tables[LOOKUP[o]].rearrange("(p c) d -> p (c d)", c=RCH)
                sp.dma_start(table[0:full, o, :], rows[0:full]).then_inc(s_table[o], 16)
                sp.dma_start(table[full:RP, o, :], rows[full:RP]).then_inc(s_table[o], 16)
                if o <= 1:
                    part_ids = slice(0, 1) if o == 0 else slice(1, NL)
                    sp.dma_start(want_i[:, part_ids, :].rearrange("p o b -> p (o b)"),
                                 lookup_ids[part_ids].rearrange("o b -> (o b)").partition_broadcast(RP)
                                 ).then_inc(s_want[o], 16)
                if o == 0:
                    sp.dma_start(dense_sb[:], dense.rearrange("(t p) d -> p t d", p=P)).then_inc(s_dense, 16)
                    sp.dma_start(small[0:K1, :], b1.rearrange("(k p) -> k p", p=P)).then_inc(s_small, 16)
                    sp.dma_start(small[K1:K1 + K2, :], b2.rearrange("(k p) -> k p", p=P)).then_inc(s_small, 16)
                    sp.dma_start(small[K1 + K2:NC, :],
                                 W3.rearrange("(k p) o -> k (p o)", p=P)).then_inc(s_small, 16)
            sp.dma_start(w1a[:], W1[0:D, :]).then_inc(s_w1, 16)
            sp.dma_start(w1d[:], W1[D + PAIRS:2 * D + PAIRS, :]).then_inc(s_w1, 16)
            sp.dma_start(w1z[:], W1_pairs.rearrange("k p n -> p k n")).then_inc(s_w1z, 16)
            sp.dma_start(w2[:], W2.rearrange("(k p) n -> p k n", p=P)).then_inc(s_w2, 16)
            sp.wait_ge(s_y, TILES)
            sp.dma_start(out.rearrange("b o -> o b"), y[:]).then_inc(s_out, 16)
            sp.wait_ge(s_out, 16)

        @block.gpsimd
        def _(pool):
            nc.gpsimd.memset(ident[:], 0.0).then_inc(s_zero, 1)
            nc.gpsimd.iota(rowid_i[:], pattern=[[1, RCH]], base=0, channel_multiplier=RCH).then_inc(s_iota, 1)
            pool.wait_ge(s_zero, 1)
            nc.gpsimd.affine_select(out=ident[:], in_=ident[:], compare_op=ALU.not_equal, fill=1.0, base=0,
                                    pattern=[[-1, P]], channel_multiplier=1).then_inc(s_ident, 1)
            pool.wait_ge(s_idx, 16)
            for t in range(TILES):
                for g, group in enumerate(GROUPS):
                    if t >= 2:
                        pool.wait_ge(s_tr, tr_use(t - 2, g) + 1)
                    for f in group:
                        nc.gpsimd.indirect_dma_start(
                            out=emb[:, t % 2, COL[f], :], out_offset=None, in_=tables[f],
                            in_offset=bass.IndirectOffsetOnAxis(ap=idx[:, t, f:f + 1], axis=0),
                        ).then_inc(s_emb[t][g], 16)

        @block.tensor
        def _(pe):
            def inputs():
                pe.wait_ge(s_ident, 1)
                pe.wait_ge(s_dense, 16)
                for t in range(TILES):
                    last = nc.tensor.transpose(tr_ps[0][:, t * P:(t + 1) * P], dense_sb[:, t, :], ident[:])
                last.then_inc(s_tr, 1)
                pe.wait_ge(s_small, 48)
                nc.tensor.transpose(tr_ps[1][:, 0:NC], small[:], ident[0:NC, 0:NC]).then_inc(s_tr, 1)

            def lookup(o):
                if o >= 2:
                    pe.wait_ge(s_lcopy, o - 1)
                pe.wait_ge(s_hot, o + 1)
                for k, made in enumerate((s_part0, s_part1, s_part2)):
                    pe.wait_ge(made, o + 1)
                    for c in range(RCH):
                        last = nc.tensor.matmul(mm_ps[o % 2][:, 0:B], part[k][:, o % RING, c * D:(c + 1) * D],
                                                hot[:, o % RING, c, :], start=(c == 0 and k == 0),
                                                stop=(c == RCH - 1 and k == 2))
                last.then_inc(s_look, 1)

            def group(t, g):
                u = tr_use(t, g)
                pe.wait_ge(s_emb[t][g], 16 * len(GROUPS[g]))
                pe.wait_ge(s_tra if u % 2 else s_trv, u // 2)
                for i, f in enumerate(GROUPS[g]):
                    last = nc.tensor.transpose(tr_ps[u % 2][:, i * P:(i + 1) * P], emb[:, t % 2, COL[f], :],
                                               ident[:])
                last.then_inc(s_tr, 1)

            def bank_free(t, i):
                u = t * USES + i - WORK
                if u >= 0:
                    pe.wait_ge(s_wv, copies("V", u // USES, u % USES))
                    pe.wait_ge(s_wa, copies("A", u // USES, u % USES))

            def gram_tile(t):
                u = tr_use(t, NG - 1)
                pe.wait_ge(s_trv, u // 2 + 1)
                pe.wait_ge(s_tra, (u + 1) // 2)
                pe.wait_ge(s_lcopy, NL)
                pe.wait_ge(s_pad, 1)
                for q in range(GB):
                    bank_free(t, q)
                    for i in range(CBANK):
                        s = t * P + (q * CBANK + i) * PACK
                        dst = work_bank(t, q)[:, i * P:i * P + PACK * (N - 1)]
                        last = nc.tensor.matmul(
                            dst.rearrange("p (s n) -> p s n", s=PACK),
                            xt[:, s:s + PACK, :].rearrange("p s n -> p (s n)"), xt[:, s:s + PACK, 0:N - 1],
                            start=True, stop=True)
                    last.then_inc(s_work, 1)

            def spread(t):
                pe.wait_ge(s_wv, copies("V", t, GB - 1))
                pe.wait_ge(s_wa, copies("A", t, GB - 1))
                pe.wait_ge(s_zero_col, 1)
                for b in range(SB):
                    bank_free(t, GB + b)
                    for i, (c, _, _, _) in enumerate(BLOCKS[b * CBANK:(b + 1) * CBANK]):
                        last = nc.tensor.transpose(work_bank(t, GB + b)[0:NCH * PACKS, i * P:(i + 1) * P],
                                                   gram[:, c:c + NCH, :].rearrange("p c q -> p (c q)"), ident[:])
                    last.then_inc(s_work, 1)

            def pairs(t):
                pe.wait_ge(s_wv, copies("V", t, GB + SB - 1))
                pe.wait_ge(s_wa, copies("A", t, GB + SB - 1))
                for h in range(2):
                    bank_free(t, GB + SB + h)
                    for i in range(PACK // 2):
                        at = i * NCH * PACKS
                        last = nc.tensor.transpose(work_bank(t, GB + SB + h)[0:CH, at:at + NCH * PACKS],
                                                   z[:, h * PACK // 2 + i, :], ident[0:NCH * PACKS, 0:NCH * PACKS])
                    last.then_inc(s_work, 1)

            def layer1_dense(t):
                if t == 0:
                    pe.wait_ge(s_w1sum, 1)
                    pe.wait_ge(s_lcopy, NL)
                else:
                    pe.wait_ge(s_y, t)
                for m in range(K1):
                    nc.tensor.matmul(layer1_ps(m), w1a[:, m * P:(m + 1) * P], dense_t[:, t * P:(t + 1) * P],
                                     start=(m % (K1 // 2) == 0), stop=False, skip_group_check=True)

            def layer1_pairs(t):
                if t == 0:
                    pe.wait_ge(s_w1z, 16)
                pe.wait_ge(s_wv, copies("V", t, USES - 1))
                pe.wait_ge(s_wa, copies("A", t, USES - 1))
                for m in range(K1):
                    for k in range(NCH):
                        last = nc.tensor.matmul(layer1_ps(m), w1z[:, k, m * P:(m + 1) * P],
                                                zt[:, k, :], start=False, stop=(k == NCH - 1),
                                                skip_group_check=True)
                last.then_inc(s_l1, 1)

            def layer2(t):
                if t == 0:
                    pe.wait_ge(s_w2, 16)
                pe.wait_ge(s_h1v, t + 1)
                pe.wait_ge(s_h1a, t + 1)
                for m in range(K2):
                    for k in range(K1):
                        last = nc.tensor.matmul(layer2_ps(m), w2[:, k, m * P:(m + 1) * P],
                                                h1[:, k, :], start=(k == 0), stop=(k == K1 - 1))
                last.then_inc(s_l2, 1)

            def layer3(t):
                pe.wait_ge(s_h2v, t + 1)
                pe.wait_ge(s_h2a, t + 1)
                for k in range(K2):
                    last = nc.tensor.matmul(layer3_ps, w3_col[:, k:k + 1],
                                            h2[:, k, :], start=(k == 0), stop=(k == K2 - 1))
                last.then_inc(s_l3, 1)

            inputs()
            for o in range(NL):
                lookup(o)
                if o < NG:
                    group(0, o)
            for g in range(NL, NG):
                group(0, g)
            for t in range(TILES):
                more = list(range(FILL_GROUPS)) if t + 1 < TILES else []
                gram_tile(t)
                layer1_dense(t)
                spread(t)
                if more:
                    group(t + 1, more.pop(0))
                pairs(t)
                if more:
                    group(t + 1, more.pop(0))
                layer1_pairs(t)
                if more:
                    group(t + 1, more.pop(0))
                layer2(t)
                layer3(t)
                if t + 1 < TILES:
                    for g in range(FILL_GROUPS, NG):
                        group(t + 1, g)

        @block.vector
        def _(dve):
            def rows():
                dve.wait_ge(s_iota, 1)
                nc.vector.tensor_copy(rowid[:], rowid_i[:]).then_inc(s_rowid, 1)
                dve.wait_ge(s_rowid, 1)

            def one_hot(o):
                dve.wait_ge(s_cast, o + 1)
                for c in range(RCH):
                    last = nc.vector.tensor_scalar(hot[:, o % RING, c, :], want[:, o, :], rowid[0:RP, c:c + 1],
                                                   None, ALU.is_equal)
                last.then_inc(s_hot, 1)

            def build(o):
                tab = table[:, o, :]
                if o >= RING:
                    dve.wait_ge(s_look, o - RING + 1)
                if o == 0:
                    one_hot(o)
                dve.wait_ge(s_part0, o + 1)
                nc.vector.tensor_tensor(tab, tab, part[0][:, o % RING, :], ALU.subtract).then_inc(s_rest, 1)
                if o > 0:
                    one_hot(o)
                dve.wait_ge(s_part1, o + 1)
                nc.vector.tensor_tensor(part[2][:, o % RING, :], tab, part[1][:, o % RING, :],
                                        ALU.subtract).then_inc(s_part2, 1)

            def dense_copy():
                dve.wait_ge(s_tr, 1)
                nc.vector.tensor_copy(xt[:, :, 0], tr_ps[0][:, 0:B])
                nc.vector.tensor_copy(dense_t[:], tr_ps[0][:, 0:B]).then_inc(s_trv, 1)

            def group_copy(t, g):
                u = tr_use(t, g)
                if u % 2 == 0:
                    dve.wait_ge(s_tr, u + 1)
                    group_to_xt(nc.vector.tensor_copy, t, g).then_inc(s_trv, 1)

            def gram_copy(t):
                for q in range(GB):
                    dve.wait_ge(s_work, t * USES + q + 1)
                    for j in range(PACK // 2):
                        last = gram_to_sb(nc.vector.tensor_copy, t, q, j)
                    last.then_inc(s_wv, 1)

            def spread_copy(t):
                for b in range(0, SB, 2):
                    dve.wait_ge(s_work, t * USES + GB + b + 1)
                    columns_to_z(nc.vector.tensor_copy, t, b).then_inc(s_wv, 1)

            def pairs_copy(t):
                dve.wait_ge(s_work, t * USES + GB + SB + 1)
                pairs_to_zt(nc.vector.tensor_copy, t, 0).then_inc(s_wv, 1)

            def w1_sum():
                dve.wait_ge(s_w1, 32)
                nc.vector.tensor_tensor(w1a[:], w1a[:], w1d[:], ALU.add).then_inc(s_w1sum, 1)

            def relu(out_, in_, bias):
                return nc.vector.tensor_scalar(out_, in_, bias, 0.0, ALU.add, ALU.max)

            def layer1_relu(t):
                if t == 0:
                    dve.wait_ge(s_tra, 1)
                dve.wait_ge(s_l1, t + 1)
                for m in range(K1 // 2):
                    last = relu(h1[:, m, :], layer1_ps(m), b1_col[:, m:m + 1])
                last.then_inc(s_h1v, 1)

            def layer2_relu(t):
                dve.wait_ge(s_l2, t + 1)
                for m in range(K2 // 2):
                    last = relu(h2[:, m, :], layer2_ps(m), b2_col[:, m:m + 1])
                last.then_inc(s_h2v, 1)

            rows()
            build(0)
            build(1)
            dense_copy()
            nc.vector.memset(xt[:, :, N:SLOTS], 0.0).then_inc(s_pad, 1)
            nc.vector.memset(gram[:, N - 1, :], 0.0).then_inc(s_zero_col, 1)
            for o in range(NL):
                if o + 2 < NL:
                    build(o + 2)
                if o == NL - 2:
                    w1_sum()
                if o < NG:
                    group_copy(0, o)
            for g in range(NL, NG):
                group_copy(0, g)
            for t in range(TILES):
                more = list(range(FILL_GROUPS)) if t + 1 < TILES else []
                gram_copy(t)
                spread_copy(t)
                if more:
                    group_copy(t + 1, more.pop(0))
                pairs_copy(t)
                if more:
                    group_copy(t + 1, more.pop(0))
                layer1_relu(t)
                if more:
                    group_copy(t + 1, more.pop(0))
                layer2_relu(t)
                if t + 1 < TILES:
                    for g in range(FILL_GROUPS, NG):
                        group_copy(t + 1, g)

        @block.scalar
        def _(act):
            def cast(o):
                if o <= 1:
                    act.wait_ge(s_want[o], 16)
                nc.scalar.copy(want[:, o, :], want_i[:, o, :]).then_inc(s_cast, 1)

            def build(o):
                act.wait_ge(s_table[o], 32)
                if o >= RING:
                    act.wait_ge(s_look, o - RING + 1)
                nc.scalar.copy(part[0][:, o % RING, :], table[:, o, :]).then_inc(s_part0, 1)
                cast(o)
                act.wait_ge(s_rest, o + 1)
                nc.scalar.copy(part[1][:, o % RING, :], table[:, o, :]).then_inc(s_part1, 1)

            def lookup_copy(o):
                act.wait_ge(s_look, o + 1)
                nc.scalar.copy(xt[:, :, LOOKUP[o] + 1], mm_ps[o % 2][:, 0:B]).then_inc(s_lcopy, 1)

            def group_copy(t, g):
                u = tr_use(t, g)
                if u % 2 == 1:
                    act.wait_ge(s_tr, u + 1)
                    group_to_xt(nc.scalar.copy, t, g).then_inc(s_tra, 1)

            def gram_copy(t):
                for q in range(GB):
                    act.wait_ge(s_work, t * USES + q + 1)
                    for j in range(PACK // 2, PACK):
                        last = gram_to_sb(nc.scalar.copy, t, q, j)
                    last.then_inc(s_wa, 1)

            def spread_copy(t):
                for b in range(1, SB, 2):
                    act.wait_ge(s_work, t * USES + GB + b + 1)
                    columns_to_z(nc.scalar.copy, t, b).then_inc(s_wa, 1)

            def pairs_copy(t):
                act.wait_ge(s_work, t * USES + USES)
                pairs_to_zt(nc.scalar.copy, t, 1).then_inc(s_wa, 1)

            def relu(out_, in_, bias):
                return nc.scalar.activation(out_, in_, ACT.Relu, bias=bias)

            def layer1_relu(t):
                act.wait_ge(s_l1, t + 1)
                for m in range(K1 // 2, K1):
                    last = relu(h1[:, m, :], layer1_ps(m), b1_col[:, m:m + 1])
                last.then_inc(s_h1a, 1)

            def layer2_relu(t):
                act.wait_ge(s_l2, t + 1)
                for m in range(K2 // 2, K2):
                    last = relu(h2[:, m, :], layer2_ps(m), b2_col[:, m:m + 1])
                last.then_inc(s_h2a, 1)

            def result(t):
                act.wait_ge(s_l3, t + 1)
                nc.scalar.copy(y[0:1, t * P:(t + 1) * P], layer3_ps).then_inc(s_y, 1)

            build(0)
            build(1)
            act.wait_ge(s_tr, 2)
            nc.scalar.copy(cols[:], tr_ps[1][:, 0:NC]).then_inc(s_tra, 1)
            act.wait_ge(s_tra, 1)
            for o in range(NL):
                if o + 2 < NL:
                    build(o + 2)
                lookup_copy(o)
                if o < NG:
                    group_copy(0, o)
            for g in range(NL, NG):
                group_copy(0, g)
            for t in range(TILES):
                more = list(range(FILL_GROUPS)) if t + 1 < TILES else []
                gram_copy(t)
                spread_copy(t)
                if more:
                    group_copy(t + 1, more.pop(0))
                pairs_copy(t)
                if more:
                    group_copy(t + 1, more.pop(0))
                layer1_relu(t)
                if more:
                    group_copy(t + 1, more.pop(0))
                layer2_relu(t)
                result(t)
                if t + 1 < TILES:
                    for g in range(FILL_GROUPS, NG):
                        group_copy(t + 1, g)


N_TABLES = 26


def kernel(**inputs):
    import numpy as np
    import concourse.bacc as bacc
    from concourse.bass_utils import run_bass_kernel_spmd

    nc = bacc.Bacc("TRN2", target_bir_lowering=False, num_devices=1)
    names = ["r_dense_features", "ids"] + [f"tbl_{f}" for f in range(N_TABLES)]
    names += ["W_top1", "b_top1", "W_top2", "b_top2", "W_top3"]
    arrays = {name: np.ascontiguousarray(inputs[name]) for name in names}
    arrays["lookup_ids"] = np.ascontiguousarray(arrays["ids"][:, LOOKUP].T)
    W1, D, N = arrays["W_top1"], arrays["r_dense_features"].shape[1], N_TABLES + 1
    blocks, rows = chunk_blocks(N)
    W1_pairs = np.zeros((NCH, rows, W1.shape[1]), W1.dtype)
    for q in range(NCH):
        for c0, r0, at, n in blocks:
            c = c0 + q
            first = D + c * N - c * (c + 1) // 2
            W1_pairs[q, at + c + 1 - r0:at + n] = W1[first:first + N - 1 - c]
    arrays["W1_pairs"] = W1_pairs
    aps = {name: nc.dram_tensor(f"in_{name}", a.shape, mybir.dt.from_np(a.dtype), kind="ExternalInput").ap()
           for name, a in arrays.items()}
    out = nc.dram_tensor("out", (arrays["ids"].shape[0], 1), F32, kind="ExternalOutput").ap()
    build(nc, aps["r_dense_features"], aps["ids"], aps["lookup_ids"],
          [aps[f"tbl_{f}"] for f in range(N_TABLES)],
          aps["W_top1"], aps["W1_pairs"], aps["b_top1"], aps["W_top2"], aps["b_top2"], aps["W_top3"], out)
    r = run_bass_kernel_spmd(nc, [{f"in_{name}": a for name, a in arrays.items()}], core_ids=[0])
    return r.results[0]["out"]
```

```python
from contextlib import ExitStack

import concourse.bass as bass
from concourse import mybir

F32 = mybir.dt.float32
F32R = mybir.dt.float32r
I32 = mybir.dt.int32
ALU = mybir.AluOpType
ACT = mybir.ActivationFunctionType

P = 128
LOOKUP = [0, 16, 17, 19, 20, 21, 25]
LAST = 5
ACT_CHUNKS = 1
BANK = 512
SLOTS = 32
PACK = P // SLOTS
NCH = 3
WARM = 12


def chunk_blocks(n_features):
    blocks, at = [], 0
    for c in range(0, n_features - 1, NCH):
        blocks.append((c, c + 1, at, n_features - 1 - c))
        at += n_features - 1 - c
    return blocks, at


def gather_groups(n_tables):
    groups = []
    for f in range(n_tables):
        if f in LOOKUP:
            continue
        if groups and groups[-1][-1] == f - 1 and len(groups[-1]) < BANK // P:
            groups[-1].append(f)
        else:
            groups.append([f])
    return sorted(groups, key=lambda g: -len(g))


def steps(tiles, groups, lookups, gram_banks, spread_banks):
    order = []
    for o in range(lookups):
        order.append(("lookup", 0, o))
        if o == 0:
            order.append(("inputs", 0, 0))
        if 2 <= o < groups + 2:
            order.append(("group", 0, o - 2))
    order += [("group", 0, g) for g in range(lookups - 2, groups)]
    for t in range(tiles):
        last = t == tiles - 1
        more = [("group", t + 1, g) for g in range(groups)] if not last else []
        if t == 0:
            order.append(more.pop(0))
        elif not last:
            order += [("layer2", t - 1, m) for m in range(2)]
        order += [("gram", t, q) for q in range(gram_banks // 2)]
        if t == 1:
            order.append(("build", tiles - 1, 0))
        if t and not last:
            order.append(("layer3", t - 1, 0))
        order += [("gram", t, q) for q in range(gram_banks // 2, gram_banks)]
        order.append(("dense", t, 0))
        order += [("spread", t, b) for b in range(spread_banks)]
        order += more[:1]
        if t == 1:
            order.append(("last_lookup", tiles - 1, 0))
        order += [("pairs", t, h) for h in range(2)]
        if last:
            order.append(("layer3", t - 1, 0))
        order += more[1:3]
        order += [("layer1", t, h) for h in range(2)]
        if t + 1 < tiles - 1:
            order += more[3:]
        elif not last:
            order += more[3:-2] + [("layer2", t, m) for m in range(2)] + more[-2:]
    order += [("layer2", tiles - 1, m) for m in range(2)] + [("layer3", tiles - 1, 0)]
    return order


def build(nc, dense, ids, lookup_ids, tables, W1, W1_pairs, b1, W2, b2, W3, out):
    B, D = dense.shape
    NF = len(tables)
    N = NF + 1
    TILES = B // P
    PACKS = P // PACK
    PAIRS = N * (N - 1) // 2
    BLOCKS, CH = chunk_blocks(N)
    H1, H2 = W1.shape[1], W2.shape[1]
    K1, K2 = H1 // P, H2 // P
    GROUPS = gather_groups(NF)
    NG = len(GROUPS)
    GATHERED = [f for g in GROUPS for f in g]
    COL = {f: i for i, f in enumerate(GATHERED)}
    NL = len(LOOKUP)
    LOADED = LOOKUP + [LAST]
    N_LOADED = len(LOADED)
    ROWS = tables[LOOKUP[0]].shape[0]
    RCH = -(-ROWS // P)
    VCH = RCH - ACT_CHUNKS
    RP = ROWS // RCH
    WORK = 4
    RING = 3
    CBANK = BANK // P
    GR = P - SLOTS + N - 1
    GB = PACKS // CBANK
    BANKS_OF_BLOCKS = [[0, 7], [1, 6], [2, 5, 8], [3, 4]]
    STEPS = steps(TILES, NG, NL, GB, len(BANKS_OF_BLOCKS))
    COPIED_BY = {"gram": ["VA"] * GB, "spread": ["V", "A"] * 2, "pairs": ["V", "A"], "layer2": ["V", "A"],
                 "layer3": ["A"], "last_lookup": ["V"]}
    work = [(what, t, i) for what, t, i in STEPS if what in COPIED_BY]
    NC = K1 + K2 + K2
    assert tables[LAST].shape[0] == ROWS
    assert N % NCH == 0 and CH <= P and K1 == 4 and RP * RCH == ROWS and PACKS == SLOTS and K2 == 2

    with ExitStack() as ctx:
        def sb(name, shape, dt):
            return ctx.enter_context(nc.sbuf_tensor(name, shape, dt))

        def banks(name, n):
            return [ctx.enter_context(nc.psum_tensor(f"{name}{i}", [P, BANK], F32)) for i in range(n)]

        def sem(name):
            return ctx.enter_context(nc.semaphore(name))

        ident = sb("ident", [P, P], F32)
        idx = sb("idx", [P, TILES, NF], I32)
        emb = sb("emb", [P, 2, len(GATHERED), D], F32)
        dense_sb = sb("dense_sb", [P, TILES, D], F32)
        xt = sb("xt", [P, B, SLOTS], F32)
        dense_t = sb("dense_t", [P, B], F32)
        minus_row_i = sb("minus_row_i", [P, RCH], I32)
        minus_row = sb("minus_row", [P, RCH], F32)
        apart = sb("apart", [RP, B], F32)
        want = sb("want", [RP, RING, B], I32)
        table = sb("table", [RP, RING, RCH * D], F32)
        parts = sb("parts", [RP, RING, 2, RCH * D], F32R)
        hot = sb("hot", [RP, RING, RCH, B], F32R)
        gram = sb("gram", [P, N, PACKS], F32)
        z = sb("z", [NCH * PACKS, PACK, CH], F32)
        zt = sb("zt", [CH, NCH, P], F32)
        w1a = sb("w1a", [P, H1], F32)
        w1z = sb("w1z", [CH, NCH, H1], F32)
        w1d = sb("w1d", [P, H1], F32)
        w2 = sb("w2", [P, K1, H2], F32)
        small = sb("small", [NC, P], F32)
        cols = sb("cols", [P, NC], F32)
        h1 = sb("h1", [P, K1, P], F32)
        h2 = sb("h2", [P, K2, P], F32)
        y = sb("y", [1, B], F32)

        tr_ps = banks("tr_ps", 2)
        work_ps = banks("work_ps", WORK)
        mm_ps = banks("mm_ps", 2)

        b1_col, b2_col, w3_col = cols[:, 0:K1], cols[:, K1:K1 + K2], cols[:, K1 + K2:NC]

        s_idx = sem("s_idx")
        s_dense = sem("s_dense")
        s_small = sem("s_small")
        s_w1 = sem("s_w1")
        s_w1z = sem("s_w1z")
        s_w2 = sem("s_w2")
        s_out = sem("s_out")
        s_want = [sem(f"s_want{o}") for o in range(N_LOADED)]
        s_table = [sem(f"s_table{o}") for o in range(N_LOADED)]
        s_emb = [[sem(f"s_emb{t}_{g}") for g in range(NG)] for t in range(TILES)]
        s_zero = sem("s_zero")
        s_ident = sem("s_ident")
        s_iota = sem("s_iota")
        s_pad = sem("s_pad")
        s_minus_row = sem("s_minus_row")
        s_part0 = sem("s_part0")
        s_part1 = sem("s_part1")
        s_hot = sem("s_hot")
        s_hot_act = sem("s_hot_act")
        s_apart = sem("s_apart")
        s_w1sum = sem("s_w1sum")
        s_zero_col = sem("s_zero_col")
        s_last_part0 = sem("s_last_part0")
        s_look = sem("s_look")
        s_lcopy = sem("s_lcopy")
        s_tr = sem("s_tr")
        s_tra = sem("s_tra")
        s_work = sem("s_work")
        s_wv = sem("s_wv")
        s_wa = sem("s_wa")
        s_l1 = sem("s_l1")
        s_h1v = sem("s_h1v")
        s_h1a = sem("s_h1a")

        def gathered(t, g):
            return [f for f in GROUPS[g] if t < TILES - 1 or f != LAST]

        def samples(o):
            return slice((TILES - 1) * P if LOADED[o] == LAST else 0, B)

        FIRST = 2

        def tr_use(t, g):
            return FIRST + t * NG + g

        def use(what, t, i):
            return work.index((what, t, i))

        def work_bank(what, t, i):
            return work_ps[use(what, t, i) % WORK]

        def copies(engine, u):
            return sum(engine in COPIED_BY[what][i] for what, _, i in work[:u + 1])

        def layer1_ps(m):
            return mm_ps[m // (K1 // 2)][:, m % (K1 // 2) * P:(m % (K1 // 2) + 1) * P]

        def group_to_xt(copy, t, g):
            n, f = len(GROUPS[g]), GROUPS[g][0] + 1
            copy(xt[:, t * P:(t + 1) * P, f:f + n].rearrange("p s f -> p f s"),
                 tr_ps[tr_use(t, g) % 2][:, 0:n * P].rearrange("p (f s) -> p f s", f=n)).then_inc(s_tra, 1)

        def gram_to_sb(copy, t, q, j):
            quad = slice(j * SLOTS, min((j + 1) * SLOTS, GR))
            src = work_bank("gram", t, q)[quad, :].rearrange("p (i n) -> p i n", i=CBANK)
            return copy(gram[quad, 0:N - 1, q * CBANK:(q + 1) * CBANK].rearrange("p c i -> p i c"),
                        src[:, :, j * (N - 1):(j + 1) * (N - 1)])

        def columns_to_z(copy, t, b):
            for i, block in enumerate(BANKS_OF_BLOCKS[b]):
                _, r, at, n = BLOCKS[block]
                src = work_bank("spread", t, b)[0:NCH * PACKS, i * P:(i + 1) * P].rearrange("p (j r) -> p j r", j=PACK)
                last = copy(z[:, :, at:at + n], src[:, :, r - 1:r - 1 + n])
            return last

        def pairs_to_zt(copy, t, h):
            n = PACK // 2
            src = work_bank("pairs", t, h)[0:CH, 0:n * NCH * PACKS]
            return copy(zt[:].rearrange("p k (q j) -> p j k q", j=PACK)[:, h * n:(h + 1) * n],
                        src.rearrange("p (j k q) -> p j k q", j=n, k=NCH))

        block = ctx.enter_context(nc.Block())

        @block.sync
        def _(sp):
            sp.dma_start(idx[:], ids.rearrange("(t p) f -> p t f", p=P)).then_inc(s_idx, 16)
            full = RP // 16 * 16

            def load_table(o):
                if o >= RING:
                    sp.wait_ge(s_part1, o - RING + 1)
                    sp.wait_ge(s_hot_act, (o - RING + 1) * ACT_CHUNKS)
                sp.dma_start(want[:, o % RING, :], lookup_ids[o].partition_broadcast(RP)).then_inc(s_want[o], 16)
                rows = tables[LOADED[o]].rearrange("(p c) d -> p (c d)", c=RCH)
                sp.dma_start(table[0:full, o % RING, :], rows[0:full]).then_inc(s_table[o], 16)
                sp.dma_start(table[full:RP, o % RING, :], rows[full:RP]).then_inc(s_table[o], 16)

            load_table(0)
            sp.dma_start(dense_sb[:], dense.rearrange("(t p) d -> p t d", p=P)).then_inc(s_dense, 16)
            sp.dma_start(small[0:K1, :], b1.rearrange("(k p) -> k p", p=P)).then_inc(s_small, 16)
            sp.dma_start(small[K1:K1 + K2, :], b2.rearrange("(k p) -> k p", p=P)).then_inc(s_small, 16)
            sp.dma_start(small[K1 + K2:NC, :], W3.rearrange("(k p) o -> k (p o)", p=P)).then_inc(s_small, 16)
            for o in range(1, N_LOADED):
                load_table(o)
            sp.dma_start(w1a[:], W1[0:D, :]).then_inc(s_w1, 16)
            sp.dma_start(w1d[:], W1[D + PAIRS:2 * D + PAIRS, :]).then_inc(s_w1, 16)
            sp.dma_start(w1z[:], W1_pairs.rearrange("k p n -> p k n")).then_inc(s_w1z, 16)
            sp.dma_start(w2[:], W2.rearrange("(k p) n -> p k n", p=P)).then_inc(s_w2, 16)
            sp.wait_ge(s_wa, copies("A", len(work) - 1))
            sp.dma_start(out.rearrange("b o -> o b"), y[:]).then_inc(s_out, 16)
            sp.wait_ge(s_out, 16)

        @block.gpsimd
        def _(pool):
            nc.gpsimd.memset(ident[:], 0.0).then_inc(s_zero, 1)
            nc.gpsimd.iota(minus_row_i[:], pattern=[[-1, RCH]], base=0, channel_multiplier=-RCH).then_inc(s_iota, 1)
            pool.wait_ge(s_zero, 1)
            nc.gpsimd.affine_select(out=ident[:], in_=ident[:], compare_op=ALU.not_equal, fill=1.0, base=0,
                                    pattern=[[-1, P]], channel_multiplier=1).then_inc(s_ident, 1)
            pool.wait_ge(s_idx, 16)
            for t in range(TILES):
                for g in range(NG):
                    if t >= 2:
                        pool.wait_ge(s_tr, tr_use(t - 2, g) + 1)
                    for f in gathered(t, g):
                        nc.gpsimd.indirect_dma_start(
                            out=emb[:, t % 2, COL[f], :], out_offset=None, in_=tables[f],
                            in_offset=bass.IndirectOffsetOnAxis(ap=idx[:, t, f:f + 1], axis=0),
                        ).then_inc(s_emb[t][g], 16)

        @block.tensor
        def _(pe):
            def warm():
                pe.wait_ge(s_ident, 1)
                for _ in range(WARM):
                    nc.tensor.matmul(work_ps[0][:, 0:P], ident[:], ident[:], start=True, stop=True)

            def inputs():
                pe.wait_ge(s_dense, 16)
                for t in range(TILES):
                    last = nc.tensor.transpose(tr_ps[0][:, t * P:(t + 1) * P], dense_sb[:, t, :], ident[:])
                last.then_inc(s_tr, 1)
                pe.wait_ge(s_small, 48)
                nc.tensor.transpose(tr_ps[1][:, 0:NC], small[:], ident[0:NC, 0:NC]).then_inc(s_tr, 1)

            def one_hot_made(o, c):
                if c < VCH:
                    pe.wait_ge(s_hot, o * VCH + c + 1)
                else:
                    pe.wait_ge(s_hot_act, o * ACT_CHUNKS + c - VCH + 1)

            def lookup(o):
                if o >= 2:
                    pe.wait_ge(s_lcopy, o - 1)
                for k, made in enumerate((s_part0, s_part1)):
                    pe.wait_ge(made, o + 1)
                    for c in range(RCH):
                        if k == 0:
                            one_hot_made(o, c)
                        last = nc.tensor.matmul(mm_ps[o % 2][:, 0:B], parts[:, o % RING, k, c * D:(c + 1) * D],
                                                hot[:, o % RING, c, :], start=(c == 0 and k == 0),
                                                stop=(c == RCH - 1 and k == 1))
                last.then_inc(s_look, 1)

            def last_lookup(t):
                o = N_LOADED - 1
                pe.wait_ge(s_part0, o + 1)
                pe.wait_ge(s_part1, o + 1)
                bank_free(use("last_lookup", t, 0))
                for c in range(RCH):
                    one_hot_made(o, c)
                    last = nc.tensor.matmul(
                        work_bank("last_lookup", t, 0)[:, 0:2 * D].rearrange("p (k d) -> p k d", k=2),
                        hot[:, o % RING, c, samples(o)], parts[:, o % RING, :, c * D:(c + 1) * D],
                        start=(c == 0), stop=(c == RCH - 1))
                last.then_inc(s_work, 1)

            def group(t, g):
                u = tr_use(t, g)
                pe.wait_ge(s_emb[t][g], 16 * len(gathered(t, g)))
                pe.wait_ge(s_tra, u - 1)
                if t == TILES - 1 and LAST in GROUPS[g]:
                    pe.wait_ge(s_wv, copies("V", use("last_lookup", t, 0)))
                for i, f in enumerate(GROUPS[g]):
                    last = nc.tensor.transpose(tr_ps[u % 2][:, i * P:(i + 1) * P], emb[:, t % 2, COL[f], :],
                                               ident[:])
                last.then_inc(s_tr, 1)

            def bank_free(u):
                if u >= WORK:
                    pe.wait_ge(s_wv, copies("V", u - WORK))
                    pe.wait_ge(s_wa, copies("A", u - WORK))

            def gram_bank(t, q):
                if q == 0:
                    pe.wait_ge(s_tra, tr_use(t, NG - 1) + 1)
                    pe.wait_ge(s_lcopy, NL)
                    pe.wait_ge(s_pad, 1)
                bank_free(use("gram", t, q))
                for i in range(CBANK):
                    s = t * P + (q * CBANK + i) * PACK
                    dst = work_bank("gram", t, q)[0:GR, i * P:i * P + PACK * (N - 1)]
                    rows = xt[:].rearrange("p s n -> p (s n)")[:, s * SLOTS + 1:s * SLOTS + 1 + GR]
                    last = nc.tensor.matmul(dst.rearrange("p (s n) -> p s n", s=PACK), rows,
                                            xt[:, s:s + PACK, 0:N - 1], start=True, stop=True)
                last.then_inc(s_work, 1)

            def spread(t, b):
                u = use("gram", t, GB - 1)
                pe.wait_ge(s_wv, copies("V", u))
                pe.wait_ge(s_wa, copies("A", u))
                pe.wait_ge(s_zero_col, 1)
                bank_free(use("spread", t, b))
                for i, block in enumerate(BANKS_OF_BLOCKS[b]):
                    c = BLOCKS[block][0]
                    last = nc.tensor.transpose(work_bank("spread", t, b)[0:NCH * PACKS, i * P:i * P + GR],
                                               gram[0:GR, c:c + NCH, :].rearrange("p c q -> p (c q)"),
                                               ident[0:GR, 0:GR])
                last.then_inc(s_work, 1)

            def pairs(t, h):
                u = use("spread", t, len(BANKS_OF_BLOCKS) - 1)
                pe.wait_ge(s_wv, copies("V", u))
                pe.wait_ge(s_wa, copies("A", u))
                bank_free(use("pairs", t, h))
                for i in range(PACK // 2):
                    at = i * NCH * PACKS
                    last = nc.tensor.transpose(work_bank("pairs", t, h)[0:CH, at:at + NCH * PACKS],
                                               z[:, h * PACK // 2 + i, :], ident[0:NCH * PACKS, 0:NCH * PACKS])
                last.then_inc(s_work, 1)

            def layer1_dense(t):
                if t == 0:
                    pe.wait_ge(s_w1sum, 1)
                    pe.wait_ge(s_lcopy, NL)
                else:
                    pe.wait_ge(s_h1v, 2 * t)
                    pe.wait_ge(s_h1a, 2 * t)
                for m in range(K1):
                    nc.tensor.matmul(layer1_ps(m), w1a[:, m * P:(m + 1) * P], dense_t[:, t * P:(t + 1) * P],
                                     start=(m % (K1 // 2) == 0), stop=False, skip_group_check=True)

            def layer1_pairs(t, h):
                if t == 0:
                    pe.wait_ge(s_w1z, 16)
                u = use("pairs", t, 1)
                pe.wait_ge(s_wv, copies("V", u))
                pe.wait_ge(s_wa, copies("A", u))
                for m in range(h * K1 // 2, (h + 1) * K1 // 2):
                    for k in range(NCH):
                        last = nc.tensor.matmul(layer1_ps(m), w1z[:, k, m * P:(m + 1) * P], zt[:, k, :],
                                                start=False, stop=(k == NCH - 1), skip_group_check=True)
                last.then_inc(s_l1, 1)

            def layer2(t):
                if t == 0:
                    pe.wait_ge(s_w2, 16)
                for m in range(K2):
                    bank_free(use("layer2", t, m))
                early, late = range(K1 // 2), range(K1 // 2, K1)
                for k, m in [(k, m) for k in early for m in range(K2)] + [(k, m) for m in range(K2) for k in late]:
                    if m == 0:
                        pe.wait_ge(s_h1v if k in early else s_h1a, 2 * t + k % (K1 // 2) + 1)
                    last = nc.tensor.matmul(work_bank("layer2", t, m)[:, 0:P], w2[:, k, m * P:(m + 1) * P],
                                            h1[:, k, :], start=(k == 0), stop=(k == K1 - 1))
                    if k == K1 - 1:
                        last.then_inc(s_work, 1)

            def layer3(t):
                bank_free(use("layer3", t, 0))
                for k in range(K2):
                    if k == 0:
                        pe.wait_ge(s_wv, copies("V", use("layer2", t, k)))
                    else:
                        pe.wait_ge(s_wa, copies("A", use("layer2", t, k)))
                    last = nc.tensor.matmul(work_bank("layer3", t, 0)[0:1, 0:P], w3_col[:, k:k + 1], h2[:, k, :],
                                            start=(k == 0), stop=(k == K2 - 1))
                last.then_inc(s_work, 1)

            warm()
            for what, t, i in STEPS:
                if what == "lookup":
                    lookup(i)
                elif what == "last_lookup":
                    last_lookup(t)
                elif what == "inputs":
                    inputs()
                elif what == "group":
                    group(t, i)
                elif what == "gram":
                    gram_bank(t, i)
                elif what == "dense":
                    layer1_dense(t)
                elif what == "spread":
                    spread(t, i)
                elif what == "pairs":
                    pairs(t, i)
                elif what == "layer1":
                    layer1_pairs(t, i)
                elif what == "layer2" and i == 0:
                    layer2(t)
                elif what == "layer3":
                    layer3(t)

        @block.vector
        def _(dve):
            def rows():
                dve.wait_ge(s_iota, 1)
                nc.vector.tensor_copy(minus_row[:], minus_row_i[:]).then_inc(s_minus_row, 1)
                dve.wait_ge(s_minus_row, 1)

            def one_hot(o):
                dve.wait_ge(s_want[o], 16)
                for c in range(VCH):
                    nc.vector.tensor_scalar(hot[:, o % RING, c, samples(o)], want[:, o % RING, samples(o)],
                                            minus_row[0:RP, c:c + 1], 0.0, ALU.add,
                                            ALU.is_equal).then_inc(s_hot, 1)

            def build(o):
                if o >= RING:
                    dve.wait_ge(s_look, o - RING + 1)
                one_hot(o)
                dve.wait_ge(s_part0, o + 1)
                nc.vector.tensor_tensor(parts[:, o % RING, 1, :], table[:, o % RING, :],
                                        parts[:, o % RING, 0, :].bitcast(F32), ALU.subtract).then_inc(s_part1, 1)

            def last_lookup_sum(t):
                group = next(g for g in range(NG) if LAST in GROUPS[g])
                dve.wait_ge(s_tr, tr_use(t - 2, group) + 1)
                dve.wait_ge(s_work, use("last_lookup", t, 0) + 1)
                rows = work_bank("last_lookup", t, 0)
                place = emb[:, t % 2, COL[LAST], :]
                nc.vector.tensor_copy(place, rows[:, 0:D]).then_inc(s_last_part0, 1)
                dve.wait_ge(s_last_part0, 1)
                nc.vector.tensor_tensor(place, place, rows[:, D:2 * D], ALU.add).then_inc(s_wv, 1)

            def gram_copy(t, q):
                dve.wait_ge(s_work, use("gram", t, q) + 1)
                for j in range(PACK // 2):
                    last = gram_to_sb(nc.vector.tensor_copy, t, q, j)
                last.then_inc(s_wv, 1)

            def spread_copy(t, b):
                dve.wait_ge(s_work, use("spread", t, b) + 1)
                columns_to_z(nc.vector.tensor_copy, t, b).then_inc(s_wv, 1)

            def pairs_copy(t):
                dve.wait_ge(s_work, use("pairs", t, 0) + 1)
                pairs_to_zt(nc.vector.tensor_copy, t, 0).then_inc(s_wv, 1)

            def w1_sum():
                dve.wait_ge(s_w1, 32)
                nc.vector.tensor_tensor(w1a[:], w1a[:], w1d[:], ALU.add).then_inc(s_w1sum, 1)

            def relu(out_, in_, bias):
                return nc.vector.tensor_scalar(out_, in_, bias, 0.0, ALU.add, ALU.max)

            def layer1_relu(t):
                if t == 0:
                    dve.wait_ge(s_tra, FIRST)
                dve.wait_ge(s_l1, 2 * t + 1)
                for m in range(K1 // 2):
                    relu(h1[:, m, :], layer1_ps(m), b1_col[:, m:m + 1]).then_inc(s_h1v, 1)

            def layer2_relu(t):
                dve.wait_ge(s_work, use("layer2", t, 0) + 1)
                relu(h2[:, 0, :], work_bank("layer2", t, 0)[:, 0:P], b2_col[:, 0:1]).then_inc(s_wv, 1)

            rows()
            nc.vector.memset(xt[:, :, N:SLOTS], 0.0).then_inc(s_pad, 1)
            build(0)
            build(1)
            nc.vector.memset(gram[:, N - 1, :], 0.0).then_inc(s_zero_col, 1)
            for what, t, i in STEPS:
                if what == "lookup" and i + 2 < NL:
                    build(i + 2)
                elif what == "lookup" and i == NL - 1:
                    w1_sum()
                elif what == "build":
                    build(N_LOADED - 1)
                elif (what, t, i) == ("group", TILES - 1, NG - 1):
                    dve.wait_ge(s_tr, tr_use(t, i) + 1)
                    group_to_xt(nc.vector.tensor_copy, t, i)
                elif what == "last_lookup":
                    last_lookup_sum(t)
                elif what == "gram":
                    gram_copy(t, i)
                elif what == "spread" and i % 2 == 0:
                    spread_copy(t, i)
                elif what == "pairs" and i == 0:
                    pairs_copy(t)
                elif what == "layer1" and i == 0:
                    layer1_relu(t)
                elif what == "layer2" and i == 0:
                    layer2_relu(t)

        @block.scalar
        def _(act):
            def build(o):
                act.wait_ge(s_table[o], 32)
                if o >= RING:
                    act.wait_ge(s_look, o - RING + 1)
                nc.scalar.copy(parts[:, o % RING, 0, :], table[:, o % RING, :]).then_inc(s_part0, 1)
                act.wait_ge(s_want[o], 16)
                if o == 0:
                    act.wait_ge(s_minus_row, 1)
                for c in range(VCH, RCH):
                    done = o * ACT_CHUNKS + c - VCH
                    if done:
                        act.wait_ge(s_hot_act, done)
                    nc.scalar.activation(apart[:, samples(o)], want[:, o % RING, samples(o)], ACT.Abs,
                                         bias=minus_row[0:RP, c:c + 1]).then_inc(s_apart, 1)
                    act.wait_ge(s_apart, done + 1)
                    nc.scalar.activation(hot[:, o % RING, c, samples(o)], apart[:, samples(o)], ACT.Relu, bias=1.0,
                                         scale=-1.0).then_inc(s_hot_act, 1)

            def lookup_copy(o):
                act.wait_ge(s_look, o + 1)
                nc.scalar.copy(xt[:, :, LOOKUP[o] + 1], mm_ps[o % 2][:, 0:B]).then_inc(s_lcopy, 1)

            def inputs_copy():
                act.wait_ge(s_tr, 1)
                nc.scalar.copy(xt[:, :, 0], tr_ps[0][:, 0:B])
                nc.scalar.copy(dense_t[:], tr_ps[0][:, 0:B]).then_inc(s_tra, 1)
                act.wait_ge(s_tr, 2)
                nc.scalar.copy(cols[:], tr_ps[1][:, 0:NC]).then_inc(s_tra, 1)
                act.wait_ge(s_tra, 2)

            def gram_copy(t, q):
                act.wait_ge(s_work, use("gram", t, q) + 1)
                for j in range(PACK // 2, PACK):
                    last = gram_to_sb(nc.scalar.copy, t, q, j)
                last.then_inc(s_wa, 1)

            def spread_copy(t, b):
                act.wait_ge(s_work, use("spread", t, b) + 1)
                columns_to_z(nc.scalar.copy, t, b).then_inc(s_wa, 1)

            def pairs_copy(t):
                act.wait_ge(s_work, use("pairs", t, 1) + 1)
                pairs_to_zt(nc.scalar.copy, t, 1).then_inc(s_wa, 1)

            def relu(out_, in_, bias):
                return nc.scalar.activation(out_, in_, ACT.Relu, bias=bias)

            def layer1_relu(t):
                act.wait_ge(s_l1, 2 * t + 2)
                for m in range(K1 // 2, K1):
                    relu(h1[:, m, :], layer1_ps(m), b1_col[:, m:m + 1]).then_inc(s_h1a, 1)

            def layer2_relu(t):
                act.wait_ge(s_work, use("layer2", t, 1) + 1)
                relu(h2[:, 1, :], work_bank("layer2", t, 1)[:, 0:P], b2_col[:, 1:2]).then_inc(s_wa, 1)

            def result(t):
                act.wait_ge(s_work, use("layer3", t, 0) + 1)
                nc.scalar.copy(y[0:1, t * P:(t + 1) * P], work_bank("layer3", t, 0)[0:1, 0:P]).then_inc(s_wa, 1)

            build(0)
            build(1)
            for what, t, i in STEPS:
                if what == "lookup":
                    if i + 2 < NL:
                        build(i + 2)
                    lookup_copy(i)
                elif what == "build":
                    build(N_LOADED - 1)
                elif what == "inputs":
                    inputs_copy()
                elif what == "group" and (t, i) != (TILES - 1, NG - 1):
                    act.wait_ge(s_tr, tr_use(t, i) + 1)
                    group_to_xt(nc.scalar.copy, t, i)
                elif what == "gram":
                    gram_copy(t, i)
                elif what == "spread" and i % 2 == 1:
                    spread_copy(t, i)
                elif what == "pairs" and i == 1:
                    pairs_copy(t)
                elif what == "layer1" and i == 1:
                    layer1_relu(t)
                elif what == "layer2" and i == 1:
                    layer2_relu(t)
                elif what == "layer3":
                    result(t)


N_TABLES = 26


def kernel(**inputs):
    import numpy as np
    import concourse.bacc as bacc
    from concourse.bass_utils import run_bass_kernel_spmd

    nc = bacc.Bacc("TRN2", target_bir_lowering=False, num_devices=1)
    names = ["r_dense_features", "ids"] + [f"tbl_{f}" for f in range(N_TABLES)]
    names += ["W_top1", "b_top1", "W_top2", "b_top2", "W_top3"]
    arrays = {name: np.ascontiguousarray(inputs[name]) for name in names}
    arrays["lookup_ids"] = np.ascontiguousarray(arrays["ids"][:, LOOKUP + [LAST]].T)
    W1, D, N = arrays["W_top1"], arrays["r_dense_features"].shape[1], N_TABLES + 1
    blocks, rows = chunk_blocks(N)
    W1_pairs = np.zeros((NCH, rows, W1.shape[1]), W1.dtype)
    for q in range(NCH):
        for c0, r0, at, n in blocks:
            c = c0 + q
            first = D + c * N - c * (c + 1) // 2
            W1_pairs[q, at + c + 1 - r0:at + n] = W1[first:first + N - 1 - c]
    arrays["W1_pairs"] = W1_pairs
    aps = {name: nc.dram_tensor(f"in_{name}", a.shape, mybir.dt.from_np(a.dtype), kind="ExternalInput").ap()
           for name, a in arrays.items()}
    out = nc.dram_tensor("out", (arrays["ids"].shape[0], 1), F32, kind="ExternalOutput").ap()
    build(nc, aps["r_dense_features"], aps["ids"], aps["lookup_ids"],
          [aps[f"tbl_{f}"] for f in range(N_TABLES)],
          aps["W_top1"], aps["W1_pairs"], aps["b_top1"], aps["W_top2"], aps["b_top2"], aps["W_top3"], out)
    r = run_bass_kernel_spmd(nc, [{f"in_{name}": a for name, a in arrays.items()}], core_ids=[0])
    return r.results[0]["out"]
```
